# Optimizing a Trainium2 kernel written in Bass

```python
import numpy as np
import jax
import jax.numpy as jnp

def _softmax(x, axis=-1):
    return jax.nn.softmax(x, axis=axis)

def _gelu(x):
    return jax.nn.gelu(x, approximate=True)

def _silu(x):
    return jax.nn.silu(x)

def _sigmoid(x):
    return jax.nn.sigmoid(x)

def _layernorm(x, axis=-1, eps=1e-05):
    m = jnp.mean(x, axis=axis, keepdims=True)
    v = jnp.var(x, axis=axis, keepdims=True)
    return (x - m) / jnp.sqrt(v + eps)

def _scatter_add(tgt, idx, src, axis=0):
    return tgt.at[idx].add(src)

def _segment_sum(src, seg, n):
    return jax.ops.segment_sum(src, seg, n)
kernel_name = 'mk_gnn_preln_d4_gnn_r32_ae3c6d'

def setup_inputs(seed: int=0):
    np.random.seed(seed)
    _w = jnp.asarray

    def _rec_inputs():
        import jax
        import jax.numpy as jnp
        _gk = jax.random.key(seed)
        x = -0.0005121 + 1.001 * jax.random.normal(jax.random.fold_in(_gk, 1), (3125, 32), jnp.float32)
        src = jax.random.randint(jax.random.fold_in(_gk, 2), (100000,), 0, 3125, jnp.int32)
        dst = jax.random.randint(jax.random.fold_in(_gk, 3), (100000,), 0, 3125, jnp.int32)
        _o = jnp.argsort(dst, stable=True)
        src = src[_o]
        dst = dst[_o]
        edge_attr_3 = -0.000451519 + 1.00018 * jax.random.normal(jax.random.fold_in(_gk, 13), (100000, 3), jnp.float32)
        edge_attr_32 = 0.000189758 + 1.00013 * jax.random.normal(jax.random.fold_in(_gk, 14), (100000, 32), jnp.float32)
        return (x, src, dst, edge_attr_3, edge_attr_32)
    x, src, dst, edge_attr_3, edge_attr_32 = _rec_inputs()

    def _L0_gnn_setup():
        import jax, jax.numpy as jnp
        import numpy as np
        N_NODES = 3125
        N_EDGES = 50000
        D_FEAT = 32
        EPS = 1e-12
        key = jax.random.key(seed)
        k1, k2, k3 = jax.random.split(key, 3)
        feat = jax.random.normal(k1, (N_NODES, D_FEAT), dtype=jnp.float32)
        beta = jnp.ones((1,), dtype=jnp.float32)
        src = jax.random.randint(k2, (N_EDGES,), 0, N_NODES, dtype=jnp.int32)
        dst = jax.random.randint(k3, (N_EDGES,), 0, N_NODES, dtype=jnp.int32)
        return {'feat': feat, 'beta': beta, 'src': src, 'dst': dst}
    _L0_gnn_all = _L0_gnn_setup()
    _L0_gnn_in = {k: v for k, v in _L0_gnn_all.items() if k in ('beta',)}
    del _L0_gnn_all

    def _L1_gnn_setup():
        import jax, jax.numpy as jnp
        import numpy as np

        def real_sh_l3(vec):
            r = jnp.sqrt(jnp.sum(vec * vec, axis=-1, keepdims=True))
            v = vec / jnp.maximum(r, jnp.asarray(1e-12, vec.dtype))
            x, y, z = (v[:, 0], v[:, 1], v[:, 2])
            x2, y2, z2 = (x * x, y * y, z * z)
            C0 = 0.28209479177387814
            C1 = 0.4886025119029199
            Y = [jnp.full_like(x, C0), C1 * y, C1 * z, C1 * x, 1.0925484305920792 * x * y, 1.0925484305920792 * y * z, 0.31539156525252005 * (3.0 * z2 - 1.0), 1.0925484305920792 * x * z, 0.5462742152960396 * (x2 - y2), 0.5900435899266435 * y * (3.0 * x2 - y2), 2.890611442640554 * x * y * z, 0.4570457994644658 * y * (5.0 * z2 - 1.0), 0.3731763325901154 * z * (5.0 * z2 - 3.0), 0.4570457994644658 * x * (5.0 * z2 - 1.0), 1.445305721320277 * z * (x2 - y2), 0.5900435899266435 * x * (x2 - 3.0 * y2)]
            return jnp.stack(Y, axis=-1)
        key = jax.random.key(seed)
        k1, k2, k3, k4, k5 = jax.random.split(key, 5)
        n_atoms, hidden, num_irreps, out_ch = (50000, 32, 16, 32)
        n_edges = 25000
        node_features = jax.random.normal(k1, (n_atoms, hidden), dtype=jnp.float32)
        edge_vectors = jax.random.normal(k2, (n_edges, 3), dtype=jnp.float32)
        edge_index = jax.random.randint(k3, (2, n_edges), 0, n_atoms, dtype=jnp.int64)
        fan_in = hidden * num_irreps
        W = jax.random.normal(k4, (fan_in, out_ch), dtype=jnp.float32) / np.sqrt(fan_in)
        b = jax.random.normal(k5, (out_ch,), dtype=jnp.float32) * 0.01
        return {'node_features': node_features, 'edge_vectors': edge_vectors, 'edge_index': edge_index, 'W': W, 'b': b}
    _L1_gnn_all = _L1_gnn_setup()
    _L1_gnn_in = {k: v for k, v in _L1_gnn_all.items() if k in ('W', 'b')}
    del _L1_gnn_all

    def _L2_gnn_setup():
        import jax, jax.numpy as jnp
        import numpy as np
        N_NODES = 3125
        N_EDGES = 50000
        D_FEAT = 32
        K = 10
        ALPHA = 0.1
        key = jax.random.key(seed)
        k1, k2, k3 = jax.random.split(key, 3)
        feat = jax.random.normal(k1, (N_NODES, D_FEAT), dtype=jnp.float32)
        src = jax.random.randint(k2, (N_EDGES,), 0, N_NODES, dtype=jnp.int64)
        dst = jax.random.randint(k3, (N_EDGES,), 0, N_NODES, dtype=jnp.int64)
        return {'feat': feat, 'src': src, 'dst': dst}
    _L2_gnn_all = _L2_gnn_setup()
    _L2_gnn_in = {k: v for k, v in _L2_gnn_all.items() if k in ()}
    del _L2_gnn_all

    def _L3_gnn_setup():
        import jax, jax.numpy as jnp
        import numpy as np
        N_NODES = 3125
        N_EDGES = 50000
        F_NODE = 32
        F_EDGE = 32
        HID = 64
        N_TGT = 32
        key = jax.random.key(seed)
        ks = jax.random.split(key, 12)
        x = jax.random.normal(ks[0], (N_NODES, F_NODE), dtype=jnp.float32)
        edge_index = jax.random.randint(ks[1], (2, N_EDGES), 0, N_NODES, dtype=jnp.int64)
        edge_attr = jax.random.normal(ks[2], (N_EDGES, F_EDGE), dtype=jnp.float32)
        u = jax.random.normal(ks[3], (1, 8), dtype=jnp.float32)
        batch = jnp.zeros((N_NODES,), dtype=jnp.int64)
        s1 = 1.0 / np.sqrt(F_NODE + F_EDGE)
        s2 = 1.0 / np.sqrt(HID)
        s3 = 1.0 / np.sqrt(HID + F_NODE)
        W1a = jax.random.uniform(ks[4], (F_NODE + F_EDGE, HID), jnp.float32, -s1, s1)
        b1a = jax.random.uniform(ks[5], (HID,), jnp.float32, -s1, s1)
        W1b = jax.random.uniform(ks[6], (HID, HID), jnp.float32, -s2, s2)
        b1b = jax.random.uniform(ks[7], (HID,), jnp.float32, -s2, s2)
        W2a = jax.random.uniform(ks[8], (HID + F_NODE, HID), jnp.float32, -s3, s3)
        b2a = jax.random.uniform(ks[9], (HID,), jnp.float32, -s3, s3)
        W2b = jax.random.uniform(ks[10], (HID, N_TGT), jnp.float32, -s2, s2)
        b2b = jax.random.uniform(ks[11], (N_TGT,), jnp.float32, -s2, s2)
        return {'x': x, 'edge_index': edge_index, 'edge_attr': edge_attr, 'u': u, 'batch': batch, 'W1a': W1a, 'b1a': b1a, 'W1b': W1b, 'b1b': b1b, 'W2a': W2a, 'b2a': b2a, 'W2b': W2b, 'b2b': b2b}
    _L3_gnn_all = _L3_gnn_setup()
    _L3_gnn_in = {k: v for k, v in _L3_gnn_all.items() if k in ('u', 'W1a', 'b1a', 'W1b', 'b1b', 'W2a', 'b2a', 'W2b', 'b2b')}
    del _L3_gnn_all
    return {'x': x, 'src': src, 'dst': dst, 'edge_attr_3': edge_attr_3, 'edge_attr_32': edge_attr_32, 'L0_gnn_beta': _L0_gnn_in['beta'], 'L1_gnn_W': _L1_gnn_in['W'], 'L1_gnn_b': _L1_gnn_in['b'], 'L3_gnn_u': _L3_gnn_in['u'], 'L3_gnn_W1a': _L3_gnn_in['W1a'], 'L3_gnn_b1a': _L3_gnn_in['b1a'], 'L3_gnn_W1b': _L3_gnn_in['W1b'], 'L3_gnn_b1b': _L3_gnn_in['b1b'], 'L3_gnn_W2a': _L3_gnn_in['W2a'], 'L3_gnn_b2a': _L3_gnn_in['b2a'], 'L3_gnn_W2b': _L3_gnn_in['W2b'], 'L3_gnn_b2b': _L3_gnn_in['b2b']}

def reference(x, src, dst, edge_attr_3, edge_attr_32, L0_gnn_beta, L1_gnn_W, L1_gnn_b, L3_gnn_u, L3_gnn_W1a, L3_gnn_b1a, L3_gnn_W1b, L3_gnn_b1b, L3_gnn_W2a, L3_gnn_b2a, L3_gnn_W2b, L3_gnn_b2b):
    import jax
    import jax.numpy as jnp

    def _L0_gnn_ref(feat, beta, src, dst):
        import jax, jax.numpy as jnp
        import numpy as np
        N_NODES = 3125
        N_EDGES = 50000
        D_FEAT = 32
        EPS = 1e-12
        N = feat.shape[0]
        norm = jnp.maximum(jnp.linalg.norm(feat, axis=-1, keepdims=True), EPS)
        norm_h = feat / norm
        cos = jnp.sum(norm_h[src] * norm_h[dst], axis=-1)
        e = beta[0] * cos
        m = jax.lax.stop_gradient(jax.ops.segment_max(e, dst, num_segments=N))
        m = jnp.where(jnp.isfinite(m), m, 0.0)
        p = jnp.exp(e - m[dst])
        s = jax.ops.segment_sum(p, dst, num_segments=N)
        p = p / s[dst]
        out = jax.ops.segment_sum(feat[src] * p[:, None], dst, num_segments=N)
        return out

    def _L1_gnn_ref(node_features, edge_vectors, edge_index, W, b):
        import jax, jax.numpy as jnp
        import numpy as np

        def real_sh_l3(vec):
            r = jnp.sqrt(jnp.sum(vec * vec, axis=-1, keepdims=True))
            v = vec / jnp.maximum(r, jnp.asarray(1e-12, vec.dtype))
            x, y, z = (v[:, 0], v[:, 1], v[:, 2])
            x2, y2, z2 = (x * x, y * y, z * z)
            C0 = 0.28209479177387814
            C1 = 0.4886025119029199
            Y = [jnp.full_like(x, C0), C1 * y, C1 * z, C1 * x, 1.0925484305920792 * x * y, 1.0925484305920792 * y * z, 0.31539156525252005 * (3.0 * z2 - 1.0), 1.0925484305920792 * x * z, 0.5462742152960396 * (x2 - y2), 0.5900435899266435 * y * (3.0 * x2 - y2), 2.890611442640554 * x * y * z, 0.4570457994644658 * y * (5.0 * z2 - 1.0), 0.3731763325901154 * z * (5.0 * z2 - 3.0), 0.4570457994644658 * x * (5.0 * z2 - 1.0), 1.445305721320277 * z * (x2 - y2), 0.5900435899266435 * x * (x2 - 3.0 * y2)]
            return jnp.stack(Y, axis=-1)
        n_atoms = node_features.shape[0]
        sources, targets = (edge_index[0], edge_index[1])
        Y = real_sh_l3(edge_vectors)
        msg = node_features[sources][:, :, None] * Y[:, None, :]
        agg = jax.ops.segment_sum(msg, targets, num_segments=n_atoms)
        out = agg.reshape(n_atoms, -1) @ W + b
        return out

    def _L2_gnn_ref(feat, src, dst):
        import jax, jax.numpy as jnp
        import numpy as np
        N_NODES = 3125
        N_EDGES = 50000
        D_FEAT = 32
        K = 10
        ALPHA = 0.1
        n = feat.shape[0]
        ones = jnp.ones(src.shape[0], dtype=feat.dtype)
        out_deg = jax.ops.segment_sum(ones, src, num_segments=n)
        in_deg = jax.ops.segment_sum(ones, dst, num_segments=n)
        src_norm = jnp.clip(out_deg, 1.0, None) ** (-0.5)
        dst_norm = jnp.clip(in_deg, 1.0, None) ** (-0.5)
        feat0 = feat

        def step(f, _):
            f = f * src_norm[:, None]
            agg = jax.ops.segment_sum(f[src], dst, num_segments=n)
            f = agg * dst_norm[:, None]
            f = (1.0 - ALPHA) * f + ALPHA * feat0
            return (f, None)
        feat, _ = jax.lax.scan(step, feat, None, length=K)
        return feat

    def _L3_gnn_ref(x, edge_index, edge_attr, u, batch, W1a, b1a, W1b, b1b, W2a, b2a, W2b, b2b):
        import jax, jax.numpy as jnp
        import numpy as np
        N_NODES = 3125
        N_EDGES = 50000
        F_NODE = 32
        F_EDGE = 32
        HID = 64
        N_TGT = 32
        row, col = (edge_index[0], edge_index[1])
        n = x.shape[0]
        m = jnp.concatenate([x[col], edge_attr], axis=1)
        m = jax.nn.relu(m @ W1a + b1a) @ W1b + b1b
        summed = jax.ops.segment_sum(m, row, num_segments=n)
        counts = jax.ops.segment_sum(jnp.ones((m.shape[0],), m.dtype), row, num_segments=n)
        agg = summed / jnp.maximum(counts, 1.0)[:, None]
        h = jnp.concatenate([x, agg], axis=1)
        out = jax.nn.relu(h @ W2a + b2a) @ W2b + b2b
        return out
    edge_index = jnp.stack([src, dst])
    batch0 = jnp.zeros((3125,), jnp.int32)
    h = jnp.maximum(_layernorm(x, axis=-1), 0.0)
    x = x + _L0_gnn_ref(h, L0_gnn_beta, src, dst)
    h = jnp.maximum(_layernorm(x, axis=-1), 0.0)
    x = x + _L1_gnn_ref(h, edge_attr_3, edge_index, L1_gnn_W, L1_gnn_b)
    h = jnp.maximum(_layernorm(x, axis=-1), 0.0)
    x = x + _L2_gnn_ref(h, src, dst)
    h = jnp.maximum(_layernorm(x, axis=-1), 0.0)
    x = x + _L3_gnn_ref(h, edge_index, edge_attr_32, L3_gnn_u, batch0, L3_gnn_W1a, L3_gnn_b1a, L3_gnn_W1b, L3_gnn_b1b, L3_gnn_W2a, L3_gnn_b2a, L3_gnn_W2b, L3_gnn_b2b)
    return x

_drawn_inputs = setup_inputs


def setup_inputs(seed=0):
    import zlib

    import numpy as np

    out = dict(_drawn_inputs(seed))
    spreads = {}
    factors = {'edge_attr_32': 8.0,
     'L1_gnn_b': 22.969,
     'L3_gnn_W1a': 8.0,
     'L3_gnn_b1a': 8.0,
     'L3_gnn_W1b': 4.961,
     'L3_gnn_b1b': 8.0,
     'L3_gnn_b2a': 11.913,
     'L3_gnn_b2b': 3.952}
    for name, (base, spread) in spreads.items():
        noise = np.random.default_rng([zlib.crc32(name.encode()), seed]).standard_normal(out[name].shape)
        drawn = base * np.exp(spread * noise) if base else spread * noise
        out[name] = jnp.asarray(drawn.astype(out[name].dtype))
    for name, factor in factors.items():
        out[name] = (out[name] * factor).astype(out[name].dtype)
    return out
```

```python
import concourse.bass as bass
from concourse import mybir
from contextlib import ExitStack

F32 = mybir.dt.float32
BF16 = mybir.dt.bfloat16
I32 = mybir.dt.int32
I16 = mybir.dt.int16
ALU = mybir.AluOpType
ACT = mybir.ActivationFunctionType
X = mybir.AxisListType.X
RMAX = bass.bass_isa.ReduceOp.max

P = 128
NODES, EDGES, D = 3125, 100000, 32
NB = -(-NODES // P)
NP = NB * P
GT = 4
KR, Q = 7, 112
T = KR * Q
EP = T * P
G = T // GT
HID, NSH = 64, 16
STEPS, ALPHA = 10, 0.1
PAY = D + 2
BANK = 512
CHUNKS = [(c, min(BANK, NP - c)) for c in range(0, NP, BANK)]
BIG = 1.0e38
EPS = 1e-5
DLO, DHI, SLO, SHI = range(4)
SH1, SH2 = 0.4886025119029199, 1.0925484305920792


def take(eng, sem, n=1):
    eng.wait_ge(sem, n)
    eng.sem_inc(sem, -n)


def chain(eng, sem):
    def step(ins):
        ins.then_inc(sem, 1)
        take(eng, sem)
    return step


def per_node(col, width=D):
    return col.unsqueeze(2).to_broadcast([P, NB, width])


class Mem:
    pass


class Step:
    def __init__(self, nc, eng, s_done, s_asked, s_rooted):
        self.nc, self.eng, self.s_done, self.s_asked, self.s_rooted = nc, eng, s_done, s_asked, s_rooted

    def run(self, ins):
        ins.then_inc(self.s_done, 1)
        take(self.eng, self.s_done)

    def rsqrt(self, out, v, root, t):
        vec = self.nc.vector
        self.eng.sem_inc(self.s_asked, 1)
        take(self.eng, self.s_rooted)
        self.run(vec.reciprocal(out, root))
        self.run(vec.tensor_tensor(t, out, out, ALU.mult))
        self.run(vec.tensor_tensor(t, t, v, ALU.mult))
        self.run(vec.tensor_scalar(t, t, -0.5, 1.5, ALU.mult, ALU.add))
        self.run(vec.tensor_tensor(out, out, t, ALU.mult))

    def layernorm_relu(self, m):
        vec, run = self.nc.vector, self.run
        mean, var, h, sq = m.mean[:, :], m.var[:, :], m.h[:, :, :], m.sq[:, :, :]
        run(vec.tensor_reduce(mean, m.x[:, :, :], X, ALU.add))
        run(vec.tensor_scalar(mean, mean, 1.0 / D, None, ALU.mult))
        run(vec.tensor_tensor(h, m.x[:, :, :], per_node(mean), ALU.subtract))
        run(vec.tensor_tensor(sq, h, h, ALU.mult))
        run(vec.tensor_reduce(var, sq, X, ALU.add))
        run(vec.tensor_scalar(var, var, 1.0 / D, EPS, ALU.mult, ALU.add))
        self.rsqrt(m.inv[:, :], var, m.root[:, :], m.t25[:, :])
        run(vec.tensor_tensor(h, h, per_node(m.inv[:, :]), ALU.mult))
        run(vec.tensor_scalar(h, h, 0.0, None, ALU.max))


def answer_root(nc, act, s_asked, s_rooted, root, v):
    take(act, s_asked)
    nc.scalar.activation(root, v, ACT.Sqrt).then_inc(s_rooted, 1)


def setup_phase(nc, m, a):
    with ExitStack() as ctx:
        def sb(name, shape, dt):
            return ctx.enter_context(nc.sbuf_tensor(f"setu_{name}", shape, dt))

        def sem(name):
            return ctx.enter_context(nc.semaphore(f"setu_{name}"))

        rows_i = sb("rows_i", [Q, 2, KR, P], I32)
        rows_f = sb("rows_f", [Q, 2, KR, P], F32)
        rows_v = sb("rows_v", [Q, KR, P * 3], F32)
        vec = sb("vec", [P, 3, T], F32)
        sh = sb("sh", [P, T, NSH], F32)
        w = sb("w", [P, 8, T], F32)
        tri = sb("tri", [P, P], F32)
        ones = sb("ones", [P, P], F32)
        tmax = sb("tmax", [Q, KR], F32)
        tmin = sb("tmin", [Q, KR], F32)
        gi = sb("gi", [Q, KR], I32)
        gf = sb("gf", [Q, KR], F32)
        gl = sb("gl", [Q, KR], F32)
        blk = sb("blk", [P, 3, NB], F32)
        cmp = sb("cmp", [Q, 2, NB, KR], F32)
        rng = sb("rng", [P, 2, NB], F32)
        rngm = sb("rngm", [P, 2, NB], F32)
        tabf = sb("tabf", [P, 4, NB], F32)
        tabi = sb("tabi", [P, 2, NB], I32)
        src16 = sb("src16", [P, T], I16)
        blk16 = sb("blk16", [P, T], I16)
        mask = sb("mask", [P, T], I16)
        one16 = sb("one16", [P, T], BF16)
        run_ = sb("run", [P, T], F32)
        posf = sb("posf", [P, T], F32)
        cnt = sb("cnt", [P, NB], F32)
        tot = sb("tot", [P, NB], F32)
        end = sb("end", [P, NB], F32)
        first = sb("first", [P, NB], F32)
        nq = sb("nq", [P, NB, D], F32)
        ps = [ctx.enter_context(nc.psum_tensor(f"setu_turn{i}", [P, 8, P], F32)) for i in range(2)]
        pp = ctx.enter_context(nc.psum_tensor("setu_pp", [P, 2, NB], F32))

        s_x, s_idx, s_vec, s_w, s_y = sem("s_x"), sem("s_idx"), sem("s_vec"), sem("s_w"), sem("s_y")
        s_const, s_step, s_rows, s_pool = sem("s_const"), sem("s_step"), sem("s_rows"), sem("s_pool")
        s_turned, s_q, s_qread = sem("s_turned"), sem("s_q"), sem("s_qread")
        s_read = [sem(f"s_read{i}") for i in range(2)]
        s_cnt, s_pref, s_rng, s_red = sem("s_cnt"), sem("s_pref"), sem("s_rng"), sem("s_red")
        s_asked, s_rooted, s_nq, s_sh = sem("s_asked"), sem("s_rooted"), sem("s_nq"), sem("s_sh")
        BATCH = 8

        block = ctx.enter_context(nc.Block())

        @block.sync
        def _(sp):
            for i, idx in enumerate((a.dst, a.src)):
                sp.dma_start(rows_i[:, i], idx.rearrange("(k q c) -> q k c", q=Q, c=P)).then_inc(s_idx, 16)
            sp.dma_start(rows_v[:, :, :], a.vec.rearrange("(k q c) d -> q k (c d)", q=Q, c=P)).then_inc(s_vec, 16)
            sp.dma_start(m.x[:, :, :], a.x.rearrange("(h p) c -> p h c", p=P)).then_inc(s_x, 16)
            sp.dma_start(m.beta[:, :], a.beta.rearrange("(a b) -> a b", a=1).to_broadcast([D, 1])).then_inc(s_w, 16)
            sp.wait_ge(s_sh, 1)
            sp.dma_start(a.sh, sh[:, :, :].rearrange("p t k -> p (t k)")).then_inc(s_y, 16)
            sp.wait_ge(s_w, 16)
            sp.wait_ge(s_y, 16)

        @block.gpsimd
        def _(pool):
            for t in (m.ident, m.identb):
                pool.memset(t[:, :], 0.0).then_inc(s_pool, 1)
            for t in (tri, ones, m.ones, one16):
                pool.memset(t[:, :], 1.0).then_inc(s_pool, 1)
            pool.memset(m.zero[:, :], 0.0).then_inc(s_pool, 1)
            pool.wait_ge(s_pool, 7)
            for t in (m.ident, m.identb):
                pool.affine_select(out=t[:, :], in_=t[:, :], compare_op=ALU.not_equal, fill=1.0, base=0,
                                   pattern=[[-1, P]], channel_multiplier=1).then_inc(s_const, 1)
            pool.affine_select(out=tri[:, :], in_=tri[:, :], compare_op=ALU.is_gt, fill=0.0, base=0,
                               pattern=[[1, P]], channel_multiplier=-1).then_inc(s_const, 1)
            pool.iota(m.cols[:, :], [[1, NP]], base=0, channel_multiplier=0,
                      allow_small_or_imprecise_dtypes=True).then_inc(s_const, 1)
            for i, (mul, base) in enumerate(((P, 0), (P, P - 1), (1, 0))):
                pool.iota(blk[:, i, :], [[mul, NB]], base=base, channel_multiplier=0,
                          allow_small_or_imprecise_dtypes=True).then_inc(s_const, 1)
            pool.iota(gi[:, :], [[Q, KR]], base=0, channel_multiplier=1).then_inc(s_const, 1)
            pool.wait_ge(s_rng, 1)
            pool.partition_all_reduce(rngm[:, :, :].rearrange("p a b -> p (a b)"),
                                      rng[:, :, :].rearrange("p a b -> p (a b)"), P, RMAX).then_inc(s_red, 1)

        @block.tensor
        def _(pe):
            pe.wait_ge(s_const, 8)
            pe.wait_ge(s_rows, 1)
            for i in range(5):
                if i == 2:
                    pe.wait_ge(s_vec, 16)
                if i >= 2:
                    take(pe, s_read[i % 2])
                src = rows_f[:, i] if i < 2 else rows_v[:, :, :].rearrange("q k (c d) -> q k c d", d=3)[:, :, :, i - 2]
                for k in range(KR):
                    last = nc.tensor.transpose(ps[i % 2][:, k, 0:Q], src[:, k, :], m.ident[0:Q, 0:Q])
                last.then_inc(s_turned, 1)
            pe.wait_ge(s_cnt, 1)
            nc.tensor.matmul(pp[:, 0, :], tri[:, :], cnt[:, :], start=True, stop=True)
            nc.tensor.matmul(pp[:, 1, :], ones[:, :], cnt[:, :], start=True, stop=True).then_inc(s_pref, 1)
            pe.wait_ge(s_nq, 1)
            for n, b0 in enumerate(range(0, NB, BATCH)):
                take(pe, s_read[n] if n < 2 else s_qread)
                for b in range(b0, min(NB, b0 + BATCH)):
                    last = nc.tensor.transpose(ps[n % 2][0:D, b - b0, :], nq[:, b, :], m.ident[:, :])
                last.then_inc(s_q, 1)

        @block.scalar
        def _(act):
            answer_root(nc, act, s_asked, s_rooted, w[:, 2, :], w[:, 0, :])
            answer_root(nc, act, s_asked, s_rooted, m.root[:, :], m.var[:, :])
            answer_root(nc, act, s_asked, s_rooted, m.root[:, :], m.var[:, :])
            for n, b0 in enumerate(range(0, NB, BATCH)):
                take(act, s_q)
                k = min(NB, b0 + BATCH) - b0
                nc.scalar.activation(m.nT[:, b0 * P:(b0 + k) * P], ps[n % 2][0:D, 0:k, :].rearrange("p k c -> p (k c)"),
                                     ACT.Copy).then_inc(s_qread, 1)

        @block.vector
        def _(dve):
            st = Step(nc, dve, s_step, s_asked, s_rooted)
            run, v = st.run, nc.vector
            dve.wait_ge(s_idx, 32)
            run(v.tensor_copy(rows_f[:, :, :, :].rearrange("q i k c -> q (i k c)"),
                              rows_i[:, :, :, :].rearrange("q i k c -> q (i k c)")))
            dve.sem_inc(s_rows, 1)
            v.tensor_reduce(tmax[:, :], rows_f[:, 0], X, ALU.max)
            v.tensor_reduce(tmin[:, :], rows_f[:, 0], X, ALU.min)
            for i in range(5):
                take(dve, s_turned)
                to = m.ends[:, :, i] if i < 2 else vec[:, i - 2, :]
                run(v.tensor_copy(to.rearrange("p (k q) -> p k q", q=Q), ps[i % 2][:, 0:KR, 0:Q]))
                dve.sem_inc(s_read[i % 2], 1)
            dve.wait_ge(s_const, 8)
            run(v.tensor_scalar(gi[:, :], gi[:, :], 2, None, ALU.logical_shift_right))
            run(v.tensor_copy(gf[:, :], gi[:, :]))
            run(v.tensor_scalar(gl[:, :], gf[:, :], -1.0, float(G), ALU.mult, ALU.add))
            run(v.tensor_scalar(gf[:, :], gf[:, :], 1.0, None, ALU.add))
            for i, (t, op) in enumerate(((tmax, ALU.is_ge), (tmin, ALU.is_le))):
                v.tensor_tensor(cmp[:, i], t[:, :].unsqueeze(1).to_broadcast([Q, NB, KR]),
                                blk[0:Q, i, :].unsqueeze(2).to_broadcast([Q, NB, KR]), op)
            run(v.memset(rng[:, :, :], 0.0))
            for i, t in enumerate((gl, gf)):
                run(v.tensor_tensor(cmp[:, i], cmp[:, i], t[:, :].unsqueeze(1).to_broadcast([Q, NB, KR]), ALU.mult))
            for i in range(2):
                run(v.tensor_reduce(rng[0:Q, i, :], cmp[:, i], X, ALU.max))
            dve.sem_inc(s_rng, 1)
            x, y, z = vec[:, 0, :], vec[:, 1, :], vec[:, 2, :]
            ssq, t, root, inv, x2, y2, z2, u = (w[:, i, :] for i in range(8))
            run(v.tensor_tensor(x2, x, x, ALU.mult))
            run(v.tensor_tensor(y2, y, y, ALU.mult))
            run(v.tensor_tensor(z2, z, z, ALU.mult))
            run(v.tensor_tensor(ssq, x2, y2, ALU.add))
            run(v.tensor_tensor(ssq, ssq, z2, ALU.add))
            run(v.tensor_scalar(ssq, ssq, 1e-24, None, ALU.max))
            st.rsqrt(inv, ssq, root, t)
            for c in (x, y, z):
                run(v.tensor_tensor(c, c, inv, ALU.mult))
            for c, c2 in ((x, x2), (y, y2), (z, z2)):
                run(v.tensor_tensor(c2, c, c, ALU.mult))
            v.memset(sh[:, :, 0], 0.28209479177387814)
            for k, c in ((1, y), (2, z), (3, x)):
                v.tensor_scalar(sh[:, :, k], c, SH1, None, ALU.mult)
            for k, c, e in ((4, x, y), (5, y, z), (7, x, z)):
                v.scalar_tensor_tensor(sh[:, :, k], c, SH2, e, ALU.mult, ALU.mult)
            v.tensor_scalar(sh[:, :, 6], z2, 3.0 * 0.31539156525252005, -0.31539156525252005, ALU.mult, ALU.add)
            run(v.tensor_tensor(t, x2, y2, ALU.subtract))
            v.tensor_scalar(sh[:, :, 8], t, 0.5462742152960396, None, ALU.mult)
            v.scalar_tensor_tensor(sh[:, :, 14], t, 1.445305721320277, z, ALU.mult, ALU.mult)
            run(v.scalar_tensor_tensor(u, x2, 3.0, y2, ALU.mult, ALU.subtract))
            v.scalar_tensor_tensor(sh[:, :, 9], u, 0.5900435899266435, y, ALU.mult, ALU.mult)
            run(v.scalar_tensor_tensor(t, x, 2.890611442640554, y, ALU.mult, ALU.mult))
            v.tensor_tensor(sh[:, :, 10], t, z, ALU.mult)
            run(v.tensor_scalar(u, z2, 5.0, -1.0, ALU.mult, ALU.add))
            v.scalar_tensor_tensor(sh[:, :, 11], u, 0.4570457994644658, y, ALU.mult, ALU.mult)
            v.scalar_tensor_tensor(sh[:, :, 13], u, 0.4570457994644658, x, ALU.mult, ALU.mult)
            run(v.tensor_scalar(t, z2, 5.0, -3.0, ALU.mult, ALU.add))
            v.scalar_tensor_tensor(sh[:, :, 12], t, 0.3731763325901154, z, ALU.mult, ALU.mult)
            run(v.scalar_tensor_tensor(u, y2, -3.0, x2, ALU.mult, ALU.add))
            run(v.scalar_tensor_tensor(sh[:, :, 15], u, 0.5900435899266435, x, ALU.mult, ALU.mult))
            dve.sem_inc(s_sh, 1)
            run(v.tensor_copy(src16[:, :], m.ends[:, :, 1]))
            run(v.tensor_scalar(blk16[:, :], src16[:, :], 7, None, ALU.logical_shift_right))
            with dve.Fori(0, NB) as b:
                run(v.tensor_copy(m.col[:, 0:1], blk[:, 2, bass.ds(b, 1)]))
                run(v.tensor_scalar(run_[:, :], blk16[:, :], m.col[:, 0:1], None, ALU.is_equal, ALU.add,
                                    accum_out=m.col[:, 1:2]))
                run(v.tensor_copy(cnt[:, bass.ds(b, 1)], m.col[:, 1:2]))
            dve.sem_inc(s_cnt, 1)
            dve.wait_ge(s_pref, 1)
            run(v.tensor_copy(tot[:, :], pp[:, 1, :]))
            run(v.tensor_tensor_scan(end[:, :], tot[:, :], m.zero[:, 0:NB], 0.0, ALU.add, ALU.add))
            run(v.tensor_tensor(first[:, :], end[:, :], tot[:, :], ALU.subtract))
            v.tensor_copy(tabf[:, 0, :], first[:, :])
            v.tensor_scalar(tabf[:, 1, :], end[:, :], float(GT * P - 1), None, ALU.add)
            run(v.tensor_tensor(first[:, :], first[:, :], pp[:, 0, :], ALU.add))
            run(v.tensor_scalar(first[:, :], first[:, :], -1.0, None, ALU.add))
            run(v.memset(posf[:, :], 0.0))
            with dve.Fori(0, NB) as b:
                v.tensor_copy(m.col[:, 0:1], blk[:, 2, bass.ds(b, 1)])
                run(v.tensor_copy(m.col[:, 1:2], first[:, bass.ds(b, 1)]))
                run(v.tensor_scalar(mask[:, :], blk16[:, :], m.col[:, 0:1], None, ALU.is_equal))
                run(v.tensor_tensor_scan(run_[:, :], one16[:, :], mask[:, :], m.col[:, 1:2], ALU.mult, ALU.add))
                run(v.copy_predicated(posf[:, :], mask[:, :], run_[:, :]))
            run(v.tensor_copy(m.pos[:, :], posf[:, :]))
            run(v.tensor_copy(tabi[:, :, :].rearrange("p a b -> p (a b)"), tabf[:, 0:2, :].rearrange("p a b -> p (a b)")))
            run(v.tensor_scalar(tabi[:, :, :].rearrange("p a b -> p (a b)"), tabi[:, :, :].rearrange("p a b -> p (a b)"),
                                9, None, ALU.logical_shift_right))
            run(v.tensor_copy(tabf[:, SLO:SHI + 1, :].rearrange("p a b -> p (a b)"), tabi[:, :, :].rearrange("p a b -> p (a b)")))
            dve.wait_ge(s_red, 1)
            run(v.tensor_scalar(tabf[:, DLO, :], rngm[:, 0, :], -1.0, float(G), ALU.mult, ALU.add))
            run(v.tensor_copy(tabf[:, DHI, :], rngm[:, 1, :]))
            for lo, hi in ((DLO, DHI), (SLO, SHI)):
                run(v.tensor_scalar(tabf[:, lo, :], tabf[:, lo, :], float(G - 2), None, ALU.min))
                run(v.scalar_tensor_tensor(tabf[:, hi, :], tabf[:, lo, :], 2.0, tabf[:, hi, :], ALU.add, ALU.max))
            run(v.tensor_copy(m.tab[:, :, :].rearrange("p a b -> p (a b)"), tabf[:, :, :].rearrange("p a b -> p (a b)")))
            dve.wait_ge(s_x, 16)
            st.layernorm_relu(m)
            run(v.memset(m.hw[:, :, D:D + 1], 1.0))
            run(v.tensor_copy(m.hw[:, :, 0:D], m.h[:, :, :]))
            run(v.tensor_tensor(m.sq[:, :, :], m.h[:, :, :], m.h[:, :, :], ALU.mult))
            run(v.tensor_reduce(m.var[:, :], m.sq[:, :, :], X, ALU.add))
            run(v.tensor_scalar(m.var[:, :], m.var[:, :], 1e-24, None, ALU.max))
            st.rsqrt(m.inv[:, :], m.var[:, :], m.root[:, :], m.t25[:, :])
            run(v.tensor_tensor(nq[:, :, :], m.h[:, :, :], per_node(m.inv[:, :]), ALU.mult))
            dve.sem_inc(s_nq, 1)


def adjacency_phase(nc, m, a):
    with ExitStack() as ctx:
        def sb(name, shape, dt):
            return ctx.enter_context(nc.sbuf_tensor(f"adja_{name}", shape, dt))

        def sem(name):
            return ctx.enter_context(nc.semaphore(f"adja_{name}"))

        hot_src = sb("hot_src", [P, GT, NP], BF16)
        hot_dst = sb("hot_dst", [P, GT, P], BF16)
        rel_src = sb("rel_src", [P, GT], F32)
        rel_dst = sb("rel_dst", [P, GT], F32)
        base = sb("base", [P, 1], F32)
        adj = sb("adj_rows", [P, NP], BF16)
        pay = sb("pay", [P, 2, GT, PAY], F32)
        place = sb("place", [P, 2, GT], I32)
        ps = ctx.enter_context(nc.psum_tensor("adja_adj_ps", [P, len(CHUNKS) * BANK], F32))

        s_rel, s_hot, s_hot_free, s_full = sem("s_rel"), sem("s_hot"), sem("s_hot_free"), sem("s_full")
        s_bank, s_evac, s_kept = sem("s_bank"), sem("s_evac"), sem("s_kept")
        s_loaded = [sem(f"s_loaded{i}") for i in range(2)]
        s_sorted = [sem(f"s_sorted{i}") for i in range(2)]
        s_placed = sem("s_placed")
        attr = a.attr.rearrange("(g j p) c -> g p j c", j=GT, p=P)

        block = ctx.enter_context(nc.Block())

        @block.vector
        def _(dve):
            v = nc.vector
            v.memset(base[:, :], 0.0).then_inc(s_rel, 1)
            take(dve, s_rel)
            with dve.Fori(0, NB) as b:
                lo = dve.value_load(m.tab[0:1, DLO, bass.ds(b, 1)], min_val=0, max_val=G - 2)
                hi = dve.value_load(m.tab[0:1, DHI, bass.ds(b, 1)], min_val=2, max_val=G)
                with dve.Fori(lo, hi) as g:
                    dve.drain()
                    v.tensor_copy(rel_src[:, :], m.ends[:, bass.ds(g * GT, GT), 1])
                    v.tensor_scalar(rel_dst[:, :], m.ends[:, bass.ds(g * GT, GT), 0], base[:, 0:1], None,
                                    ALU.subtract).then_inc(s_rel, 1)
                    take(dve, s_rel)
                    for j in range(GT):
                        take(dve, s_hot_free)
                        v.tensor_scalar(hot_dst[:, j, :], m.cols[:, 0:P], rel_dst[:, j:j + 1], None, ALU.is_equal)
                        v.tensor_scalar(hot_src[:, j, :], m.cols[:, :], rel_src[:, j:j + 1], None,
                                        ALU.is_equal).then_inc(s_hot, 1)
                v.tensor_scalar(base[:, :], base[:, :], float(P), None, ALU.add).then_inc(s_rel, 1)
                take(dve, s_rel)

        @block.tensor
        def _(pe):
            def tile(j, first):
                take(pe, s_hot)
                for c, n in CHUNKS:
                    if first:
                        take(pe, s_bank)
                    last = nc.tensor.matmul(ps[:, c:c + n], hot_dst[:, j, :], hot_src[:, j, c:c + n],
                                            start=first, stop=True, skip_group_check=True)
                last.then_inc(s_hot_free, 1)

            pe.sem_inc(s_hot_free, GT)
            with pe.Fori(0, NB) as b:
                lo = pe.value_load(m.tab[0:1, DLO, bass.ds(b, 1)], min_val=0, max_val=G - 2)
                hi = pe.value_load(m.tab[0:1, DHI, bass.ds(b, 1)], min_val=2, max_val=G)
                for j in range(GT):
                    tile(j, j == 0)
                with pe.Fori(lo + 1, hi):
                    for j in range(GT):
                        tile(j, False)
                pe.drain().then_inc(s_full, 1)

        @block.scalar
        def _(act):
            act.sem_inc(s_bank, len(CHUNKS))
            act.sem_inc(s_kept, 16)
            with act.Fori(0, NB) as b:
                take(act, s_kept, 16)
                take(act, s_full)
                for i, (c, n) in enumerate(CHUNKS):
                    nc.scalar.activation(adj[:, c:c + n], ps[:, c:c + n], ACT.Copy,
                                         accum_out=m.indeg7[:, bass.ds(b * len(CHUNKS) + i, 1)]).then_inc(s_bank, 1)
                act.drain().then_inc(s_evac, 1)
                take(act, s_evac)
                act.dma_start(a.adj[bass.ds(b * P, P), :], adj[:, :]).then_inc(s_kept, 16)
            take(act, s_kept, 16)

        @block.sync
        def _(sp):
            for s in range(2):
                sp.dma_start(pay[:, s, :, 0:D], attr[s]).then_inc(s_loaded[s], 16)
            done = sp.alloc_register("scattered")
            sp.reg_mov(done, 0)
            with sp.Fori(1, G // 2) as n:
                sp.reg_add(done, done, 16 * GT)
                count = sp.snap(done, min_val=16 * GT, max_val=16 * GT * G)
                for s in range(2):
                    sp.wait_ge(s_sorted[s], count)
                    sp.dma_start(pay[:, s, :, 0:D], attr[bass.ds(n * 2 + s, 1)].squeeze(0)).then_inc(s_loaded[s], 16)

        @block.gpsimd
        def _(pool):
            with pool.Fori(0, G // 2) as n:
                for s in range(2):
                    take(pool, s_loaded[s], 16)
                    pool.tensor_copy(pay[:, s, :, D:PAY], m.ends[:, bass.ds((n * 2 + s) * GT, GT), :])
                    pool.tensor_copy(place[:, s, :], m.pos[:, bass.ds((n * 2 + s) * GT, GT)]).then_inc(s_placed, 1)
                    take(pool, s_placed)
                    for j in range(GT):
                        pool.indirect_dma_start(a.sorted, bass.IndirectOffsetOnAxis(place[:, s, j:j + 1], 0),
                                                pay[:, s, j, :], None).then_inc(s_sorted[s], 16)
            for s in range(2):
                pool.wait_ge(s_sorted[s], 16 * GT * (G // 2))


def attention_phase(nc, m, a):
    with ExitStack() as ctx:
        def sb(name, shape, dt):
            return ctx.enter_context(nc.sbuf_tensor(f"atte_{name}", shape, dt))

        def sem(name):
            return ctx.enter_context(nc.semaphore(f"atte_{name}"))

        adj = sb("adj_rows", [P, NP], BF16)
        sc = sb("scores", [P, NP], F32)
        pen = sb("pen", [P, 2, BANK], BF16)
        pT = sb("pT", [P, 2, BANK], F32)
        q = sb("query", [D, P], F32)
        mx = sb("mx", [P, len(CHUNKS)], F32)
        neg = sb("neg", [P, 1], F32)
        den = sb("den", [P, 1], F32)
        ps_s = [ctx.enter_context(nc.psum_tensor(f"atte_ps_s{i}", [P, BANK], F32)) for i in range(2)]
        ps_e = [ctx.enter_context(nc.psum_tensor(f"atte_ps_e{i}", [P, BANK], F32)) for i in range(2)]
        ps_a = [ctx.enter_context(nc.psum_tensor(f"atte_ps_a{i}", [P, 2 * BANK], BF16)) for i in range(2)]
        ps_o = ctx.enter_context(nc.psum_tensor("atte_ps_o", [P, D + 1], F32))

        s_adj, s_adj_dve, s_free_pe, s_free_dve = sem("s_adj"), sem("s_adj_dve"), sem("s_free_pe"), sem("s_free_dve")
        s_q, s_s, s_s_free, s_a, s_a_free = sem("s_q"), sem("s_s"), sem("s_s_free"), sem("s_a"), sem("s_a_free")
        s_neg, s_e, s_eT, s_eT_free = sem("s_neg"), sem("s_e"), sem("s_eT"), sem("s_eT_free")
        s_p, s_p_free, s_o, s_o_free, s_step = sem("s_p"), sem("s_p_free"), sem("s_o"), sem("s_o_free"), sem("s_step")
        TB = 8
        turns = [(h, min(TB, NB - h)) for h in range(0, NB, TB)]

        block = ctx.enter_context(nc.Block())

        @block.sync
        def _(sp):
            sp.sem_inc(s_free_pe, 1)
            sp.sem_inc(s_free_dve, 1)
            with sp.Fori(0, NB) as b:
                take(sp, s_free_pe)
                take(sp, s_free_dve)
                sp.dma_start(adj[:, :], a.adj[bass.ds(b * P, P), :]).then_inc(s_adj, 16)

        @block.tensor
        def _(pe):
            def weigh(n):
                c, w = CHUNKS[n]
                take(pe, s_p)
                for i in range(w // P):
                    h = c // P + i
                    last = nc.tensor.matmul(ps_o[:, :], pT[:, n % 2, i * P:(i + 1) * P], m.hw[:, h, :],
                                            start=h == 0, stop=h == NB - 1)
                last.then_inc(s_o if n == len(CHUNKS) - 1 else s_p_free, 1)
                if n == len(CHUNKS) - 1:
                    pe.sem_inc(s_p_free, 1)

            pe.sem_inc(s_p_free, 2)
            with pe.Fori(0, NB) as b:
                take(pe, s_q)
                take(pe, s_adj, 16)
                pe.sem_inc(s_adj_dve, 1)
                for n, (c, w) in enumerate(CHUNKS):
                    take(pe, s_s_free)
                    nc.tensor.matmul(ps_s[n % 2][:, 0:w], q[:, :], m.nT[:, c:c + w], start=True,
                                     stop=True).then_inc(s_s, 1)
                    if n < len(turns):
                        h0, k = turns[n]
                        take(pe, s_a_free)
                        for i in range(k):
                            last = nc.tensor.transpose(ps_a[n % 2][:, i * P:(i + 1) * P],
                                                       adj[:, (h0 + i) * P:(h0 + i + 1) * P], m.identb[:, :])
                        last.then_inc(s_a, 1)
                pe.drain().then_inc(s_free_pe, 1)
                take(pe, s_o_free)
                for n, (c, w) in enumerate(CHUNKS):
                    take(pe, s_e)
                    take(pe, s_eT_free)
                    for i in range(w // P):
                        last = nc.tensor.transpose(ps_e[n % 2][:, i * P:(i + 1) * P],
                                                   sc[:, c + i * P:c + (i + 1) * P], m.ident[:, :])
                    last.then_inc(s_eT, 1)
                    if n:
                        weigh(n - 1)
                weigh(len(CHUNKS) - 1)

        @block.scalar
        def _(act):
            act.sem_inc(s_a_free, 2)
            with act.Fori(0, NB) as b:
                nc.scalar.activation(q[:, :], m.nT[:, bass.ds(b * P, P)], ACT.Copy,
                                     scale=m.beta[:, 0:1]).then_inc(s_q, 1)
                for n, (h0, k) in enumerate(turns):
                    take(act, s_a)
                    nc.scalar.activation(m.adjT[:, h0:h0 + k, bass.ds(b * P, P)],
                                         ps_a[n % 2][:, 0:k * P].rearrange("p (k c) -> p k c", c=P),
                                         ACT.Copy).then_inc(s_a_free, 1)
                take(act, s_neg)
                for c, w in CHUNKS:
                    nc.scalar.activation(sc[:, c:c + w], sc[:, c:c + w], ACT.Exp, bias=neg[:, 0:1]).then_inc(s_e, 1)

        @block.vector
        def _(dve):
            v = nc.vector

            def run(ins):
                ins.then_inc(s_step, 1)
                take(dve, s_step)

            dve.sem_inc(s_s_free, 2)
            dve.sem_inc(s_eT_free, 2)
            dve.sem_inc(s_o_free, 1)
            with dve.Fori(0, NB) as b:
                take(dve, s_adj_dve)
                for n, (c, w) in enumerate(CHUNKS):
                    run(v.tensor_scalar(pen[:, n % 2, 0:w], adj[:, c:c + w], 0.0, -BIG, ALU.is_equal, ALU.mult))
                    take(dve, s_s)
                    run(v.tensor_tensor_reduce(out=sc[:, c:c + w], in0=ps_s[n % 2][:, 0:w], in1=pen[:, n % 2, 0:w],
                                               scale=1.0, scalar=-3.0e38, op0=ALU.add, op1=ALU.max,
                                               accum_out=mx[:, n:n + 1]))
                    dve.sem_inc(s_s_free, 1)
                dve.sem_inc(s_free_dve, 1)
                run(v.tensor_reduce(neg[:, :], mx[:, :], X, ALU.max, negate=True))
                dve.sem_inc(s_neg, 1)
                for n, (c, w) in enumerate(CHUNKS):
                    take(dve, s_eT)
                    take(dve, s_p_free)
                    run(v.tensor_tensor(pT[:, n % 2, 0:w].rearrange("p (k c) -> p k c", c=P),
                                        ps_e[n % 2][:, 0:w].rearrange("p (k c) -> p k c", c=P),
                                        m.adjT[:, c // P:(c + w) // P, bass.ds(b * P, P)], ALU.mult))
                    dve.sem_inc(s_p, 1)
                    dve.sem_inc(s_eT_free, 1)
                take(dve, s_o)
                run(v.tensor_scalar(den[:, :], ps_o[:, D:D + 1], 0.5, None, ALU.max))
                run(v.reciprocal(den[:, :], den[:, :]))
                run(v.scalar_tensor_tensor(m.x[:, bass.ds(b, 1), :].squeeze(1), ps_o[:, 0:D], den[:, 0:1],
                                           m.x[:, bass.ds(b, 1), :].squeeze(1), ALU.mult, ALU.add))
                dve.sem_inc(s_o_free, 1)


def norm_phase(nc, m, dest, tag):
    with ExitStack() as ctx:
        s_step, s_asked, s_rooted, s_h, s_out = (ctx.enter_context(nc.semaphore(f"{tag}_{n}")) for n in
                                                 ("s_step", "s_asked", "s_rooted", "s_h", "s_out"))
        m.sq = ctx.enter_context(nc.sbuf_tensor(f"{tag}_sq", [P, NB, D], F32))
        block = ctx.enter_context(nc.Block())

        @block.vector
        def _(dve):
            Step(nc, dve, s_step, s_asked, s_rooted).layernorm_relu(m)
            dve.sem_inc(s_h, 1)

        @block.scalar
        def _(act):
            answer_root(nc, act, s_asked, s_rooted, m.root[:, :], m.var[:, :])

        @block.sync
        def _(sp):
            sp.wait_ge(s_h, 1)
            if dest is not None:
                sp.dma_start(dest.rearrange("(h p) c -> p h c", p=P), m.h[:, :, :]).then_inc(s_out, 16)
                sp.wait_ge(s_out, 16)


def convolution_phase(nc, m, a):
    with ExitStack() as ctx:
        def sb(name, shape, dt):
            return ctx.enter_context(nc.sbuf_tensor(f"conv_{name}", shape, dt))

        def sem(name):
            return ctx.enter_context(nc.semaphore(f"conv_{name}"))

        FAN = D * NSH
        KC = FAN // P
        w1 = sb("w1", [P, KC, D], F32)
        b1 = sb("b1", [1, D], F32)
        lane = sb("lane", [P, P], F32)
        src = sb("src", [P, GT], I32)
        feat = sb("feat", [P, GT, D], F32)
        sh = sb("sh", [P, 2, GT // 2, NSH], F32)
        msg = sb("msg", [P, GT, FAN], F32)
        hot = sb("hot", [P, GT, P], F32)
        rel = sb("rel", [P, GT], F32)
        base = sb("base", [P, 1], F32)
        agg = sb("agg", [P, FAN], F32)
        aggT = sb("aggT", [P, KC, P], F32)
        conv = sb("conv", [P, NB, D], F32)
        junk = sb("junk", [P, NP], BF16)
        ps_agg = ctx.enter_context(nc.psum_tensor("conv_ps_agg", [P, FAN], F32))
        ps_t = ctx.enter_context(nc.psum_tensor("conv_ps_t", [P, KC, P], F32))
        ps_o = ctx.enter_context(nc.psum_tensor("conv_ps_o", [P, D], F32))

        s_w, s_lane, s_src, s_feat_free = sem("s_w"), sem("s_lane"), sem("s_src"), sem("s_feat_free")
        s_feat = [sem(f"s_feat{j}") for j in range(GT)]
        s_sh = [sem(f"s_sh{i}") for i in range(2)]
        s_sh_free = [sem(f"s_sh_free{i}") for i in range(2)]
        s_rel, s_edge, s_edge_free, s_full = sem("s_rel"), sem("s_edge"), sem("s_edge_free"), sem("s_full")
        s_agg, s_t, s_aggT, s_o, s_done = sem("s_agg"), sem("s_t"), sem("s_aggT"), sem("s_o"), sem("s_done")

        def bounds(eng, b):
            return (eng.value_load(m.tab[0:1, DLO, bass.ds(b, 1)], min_val=0, max_val=G - 2),
                    eng.value_load(m.tab[0:1, DHI, bass.ds(b, 1)], min_val=2, max_val=G))

        block = ctx.enter_context(nc.Block())

        @block.sync
        def _(sp):
            sp.dma_start(w1[:, :, :], a.w1.rearrange("(c k) n -> k c n", c=KC)).then_inc(s_w, 16)
            sp.dma_start(b1[:, :], a.b1.rearrange("(a n) -> a n", a=1)).then_inc(s_w, 16)
            half = GT // 2 * NSH
            with sp.Fori(0, NB) as b:
                lo, hi = bounds(sp, b)
                with sp.Fori(lo, hi) as g:
                    for i in range(2):
                        take(sp, s_sh_free[i])
                        sp.dma_start(sh[:, i, :, :].rearrange("p t k -> p (t k)"),
                                     a.sh[:, bass.ds(g * (GT * NSH) + i * half, half)]).then_inc(s_sh[i], 16)

        @block.gpsimd
        def _(pool):
            pool.iota(lane[:, :], [[1, P]], base=0, channel_multiplier=0,
                      allow_small_or_imprecise_dtypes=True).then_inc(s_lane, 1)
            with pool.Fori(0, NB) as b:
                lo, hi = bounds(pool, b)
                with pool.Fori(lo, hi) as g:
                    for j in range(GT):
                        if j % 2 == 0:
                            take(pool, s_feat_free, 2)
                            pool.tensor_copy(src[:, j:j + 2], m.ends[:, bass.ds(g * GT + j, 2), 1]).then_inc(s_src, 1)
                            take(pool, s_src)
                        pool.indirect_dma_start(feat[:, j, :], None, a.h,
                                                bass.IndirectOffsetOnAxis(src[:, j:j + 1], 0)).then_inc(s_feat[j], 16)

        @block.vector
        def _(dve):
            v = nc.vector
            dve.sem_inc(s_feat_free, GT)
            for i in range(2):
                dve.sem_inc(s_sh_free[i], 1)
            v.memset(base[:, :], 0.0).then_inc(s_rel, 1)
            take(dve, s_rel)
            dve.wait_ge(s_lane, 1)
            got = dve.alloc_register("gathered")
            dve.reg_mov(got, 0)
            with dve.Fori(0, NB) as b:
                lo, hi = bounds(dve, b)
                with dve.Fori(lo, hi) as g:
                    dve.reg_add(got, got, 16)
                    count = dve.snap(got, min_val=16, max_val=16 * G * NB)
                    v.tensor_scalar(rel[:, :], m.ends[:, bass.ds(g * GT, GT), 0], base[:, 0:1], None,
                                    ALU.subtract).then_inc(s_rel, 1)
                    take(dve, s_rel)
                    for j in range(GT):
                        if j % 2 == 0:
                            take(dve, s_sh[j // 2], 16)
                        dve.wait_ge(s_feat[j], count)
                        take(dve, s_edge_free)
                        v.tensor_tensor(msg[:, j, :].rearrange("p (i k) -> p i k", k=NSH),
                                        feat[:, j, :].unsqueeze(2).to_broadcast([P, D, NSH]),
                                        sh[:, j // 2, j % 2, :].unsqueeze(1).to_broadcast([P, D, NSH]),
                                        ALU.mult).then_inc(s_feat_free, 1)
                        v.tensor_scalar(hot[:, j, :], lane[:, :], rel[:, j:j + 1], None, ALU.is_equal).then_inc(s_edge, 1)
                        if j % 2 == 1:
                            dve.drain().then_inc(s_sh_free[j // 2], 1)
                v.tensor_scalar(base[:, :], base[:, :], float(P), None, ALU.add).then_inc(s_rel, 1)
                take(dve, s_rel)
            dve.wait_ge(s_done, 1)
            v.tensor_tensor(m.x[:, :, :], m.x[:, :, :], conv[:, :, :], ALU.add)

        @block.tensor
        def _(pe):
            def tile(j, first):
                take(pe, s_edge)
                nc.tensor.matmul(ps_agg[:, :], hot[:, j, :], msg[:, j, :], start=first, stop=True,
                                 skip_group_check=True).then_inc(s_edge_free, 1)

            pe.wait_ge(s_w, 32)
            pe.sem_inc(s_edge_free, GT)
            with pe.Fori(0, NB) as b:
                lo, hi = bounds(pe, b)
                for j in range(GT):
                    tile(j, j == 0)
                with pe.Fori(lo + 1, hi):
                    for j in range(GT):
                        tile(j, False)
                pe.drain().then_inc(s_full, 1)
                take(pe, s_agg)
                for c in range(KC):
                    last = nc.tensor.transpose(ps_t[:, c, :], agg[:, c * P:(c + 1) * P], m.ident[:, :])
                last.then_inc(s_t, 1)
                take(pe, s_aggT)
                nc.tensor.matmul(ps_o[:, :], m.ones[:, :], b1[:, :], start=True, stop=False)
                for c in range(KC):
                    last = nc.tensor.matmul(ps_o[:, :], aggT[:, c, :], w1[:, c, :], start=False, stop=c == KC - 1)
                last.then_inc(s_o, 1)

        @block.scalar
        def _(act):
            with act.Fori(0, NB) as h:
                nc.scalar.activation(junk[:, :], m.adjT[:, bass.ds(h, 1), :].squeeze(1), ACT.Copy,
                                     accum_out=m.outdeg[:, bass.ds(h, 1)]).then_inc(s_done, 1)
                take(act, s_done)
            with act.Fori(0, NB) as b:
                take(act, s_full)
                nc.scalar.activation(agg[:, :], ps_agg[:, :], ACT.Copy).then_inc(s_agg, 1)
                take(act, s_t)
                nc.scalar.activation(aggT[:, :, :], ps_t[:, :, :], ACT.Copy).then_inc(s_aggT, 1)
                take(act, s_o)
                nc.scalar.activation(conv[:, bass.ds(b, 1), :].squeeze(1), ps_o[:, :], ACT.Copy)
            act.drain().then_inc(s_done, 1)


def propagation_phase(nc, m, a):
    with ExitStack() as ctx:
        def sb(name, shape, dt):
            return ctx.enter_context(nc.sbuf_tensor(f"prop_{name}", shape, dt))

        def sem(name):
            return ctx.enter_context(nc.semaphore(f"prop_{name}"))

        keep = sb("keep", [P, NB], F32)
        srcn = sb("srcn", [P, NB], F32)
        back = sb("back", [P, NB, D], F32)
        f = sb("f", [P, NB, D], F32)
        rest = sb("rest", [P, NB, D], F32)
        parts = sb("parts", [P, NB, 3 * D], BF16)
        fT = sb("fT", [3 * D, 2, BANK], F32)
        fold = sb("fold", [3 * D, D], F32)
        ps = ctx.enter_context(nc.psum_tensor("prop_ps", [P, len(CHUNKS) * BANK], F32))
        ps_n = ctx.enter_context(nc.psum_tensor("prop_ps_n", [P, BANK], F32))

        s_step, s_asked, s_rooted, s_fold = sem("s_step"), sem("s_asked"), sem("s_rooted"), sem("s_fold")
        s_parts, s_chunk, s_fT, s_nodes = sem("s_parts"), sem("s_chunk"), sem("s_fT"), sem("s_nodes")
        HALF = BANK // D
        per = BANK // P

        def nodes(h):
            return ps_n[:, h * D:(h + 1) * D] if h < HALF else ps[:, (h - HALF) * D:(h - HALF + 1) * D]

        block = ctx.enter_context(nc.Block())

        @block.gpsimd
        def _(pool):
            pool.memset(fold[:, :], 0.0).then_inc(s_fold, 1)
            pool.wait_ge(s_fold, 1)
            for i in range(3):
                part = fold[i * D:(i + 1) * D, :]
                pool.affine_select(out=part, in_=part, compare_op=ALU.not_equal, fill=1.0, base=0,
                                   pattern=[[-1, D]], channel_multiplier=1).then_inc(s_fold, 1)

        @block.scalar
        def _(act):
            answer_root(nc, act, s_asked, s_rooted, m.root[:, :], m.var[:, :])
            answer_root(nc, act, s_asked, s_rooted, m.root[:, :], m.var[:, :])
            with act.Fori(0, STEPS):
                for i, (c, n) in enumerate(CHUNKS):
                    take(act, s_chunk)
                    nc.scalar.activation(fT[:, i % 2, 0:n], ps[0:3 * D, c:c + n], ACT.Copy).then_inc(s_fT, 1)

        @block.tensor
        def _(pe):
            def fold_chunk(i):
                take(pe, s_fT)
                for k in range(CHUNKS[i][1] // P):
                    last = nc.tensor.matmul(nodes(i * per + k), fT[:, i % 2, k * P:(k + 1) * P], fold[:, :], start=True, stop=True)
                if i == len(CHUNKS) - 1:
                    last.then_inc(s_nodes, 1)

            pe.wait_ge(s_fold, 4)
            with pe.Fori(0, STEPS):
                take(pe, s_parts)
                for i, (c, n) in enumerate(CHUNKS):
                    for h in range(NB):
                        last = nc.tensor.matmul(ps[0:3 * D, c:c + n], parts[:, h, :], m.adjT[:, h, c:c + n],
                                                start=h == 0, stop=h == NB - 1)
                    last.then_inc(s_chunk, 1)
                    if i:
                        fold_chunk(i - 1)
                fold_chunk(len(CHUNKS) - 1)

        @block.vector
        def _(dve):
            st = Step(nc, dve, s_step, s_asked, s_rooted)
            run, v = st.run, nc.vector

            def split():
                for i in range(3):
                    part = parts[:, :, i * D:(i + 1) * D]
                    run(v.tensor_copy(part, rest[:, :, :]))
                    if i < 2:
                        run(v.tensor_tensor(rest[:, :, :], rest[:, :, :], part, ALU.subtract))
                dve.sem_inc(s_parts, 1)

            run(v.tensor_reduce(m.var[:, :], m.indeg7[:, :].rearrange("p (b c) -> p b c", b=NB), X, ALU.add))
            run(v.tensor_scalar(m.var[:, :], m.var[:, :], 1.0, None, ALU.max))
            st.rsqrt(keep[:, :], m.var[:, :], m.root[:, :], m.t25[:, :])
            run(v.tensor_scalar(keep[:, :], keep[:, :], 1.0 - ALPHA, None, ALU.mult))
            run(v.tensor_scalar(m.var[:, :], m.outdeg[:, :], 1.0, None, ALU.max))
            st.rsqrt(srcn[:, :], m.var[:, :], m.root[:, :], m.t25[:, :])
            run(v.tensor_scalar(back[:, :, :], m.h[:, :, :], ALPHA, None, ALU.mult))
            run(v.tensor_tensor(rest[:, :, :], m.h[:, :, :], per_node(srcn[:, :]), ALU.mult))
            split()
            with dve.Fori(0, STEPS):
                take(dve, s_nodes)
                for h0, h1, at in ((0, HALF, ps_n), (HALF, NB, ps)):
                    run(v.tensor_tensor(f[:, h0:h1, :], at[:, 0:(h1 - h0) * D].rearrange("p (h c) -> p h c", c=D),
                                        keep[:, h0:h1].unsqueeze(2).to_broadcast([P, h1 - h0, D]), ALU.mult))
                run(v.tensor_tensor(f[:, :, :], f[:, :, :], back[:, :, :], ALU.add))
                run(v.tensor_tensor(rest[:, :, :], f[:, :, :], per_node(srcn[:, :]), ALU.mult))
                split()
            v.tensor_tensor(m.x[:, :, :], m.x[:, :, :], f[:, :, :], ALU.add)


def node_half_phase(nc, m, a):
    with ExitStack() as ctx:
        def sb(name, shape, dt):
            return ctx.enter_context(nc.sbuf_tensor(f"node_{name}", shape, dt))

        def sem(name):
            return ctx.enter_context(nc.semaphore(f"node_{name}"))

        w = sb("w", [D, HID], F32)
        bias = sb("bias", [1, HID], F32)
        half = sb("half", [P, NB, HID], F32)
        ps_t = [ctx.enter_context(nc.psum_tensor(f"node_ps_t{i}", [D, BANK], F32)) for i in range(2)]
        ps_h = [ctx.enter_context(nc.psum_tensor(f"node_ps_h{i}", [P, BANK // P, HID], F32)) for i in range(2)]
        s_w, s_t, s_hT, s_h, s_h_free, s_out = (sem(n) for n in ("s_w", "s_t", "s_hT", "s_h", "s_h_free", "s_out"))
        per = BANK // P
        block = ctx.enter_context(nc.Block())

        @block.sync
        def _(sp):
            sp.dma_start(w[:, :], a.w1a[0:D, :]).then_inc(s_w, 16)
            sp.dma_start(bias[:, :], a.b1a.rearrange("(a n) -> a n", a=1)).then_inc(s_w, 16)
            sp.wait_ge(s_h_free, len(CHUNKS))
            sp.dma_start(a.half.rearrange("(h p) c -> p h c", p=P), half[:, :, :]).then_inc(s_out, 16)
            sp.wait_ge(s_out, 16)

        @block.tensor
        def _(pe):
            def product(i):
                pe.wait_ge(s_hT, i + 1)
                if i >= 2:
                    pe.wait_ge(s_h_free, i - 1)
                for k in range(CHUNKS[i][1] // P):
                    h = i * per + k
                    nc.tensor.matmul(ps_h[i % 2][:, k, :], m.hT[:, h * P:(h + 1) * P], w[:, :], start=True, stop=False)
                    last = nc.tensor.matmul(ps_h[i % 2][:, k, :], m.ones[:, :], bias[:, :], start=False, stop=True)
                last.then_inc(s_h, 1)

            pe.wait_ge(s_w, 32)
            for i, (c, n) in enumerate(CHUNKS):
                if i >= 2:
                    pe.wait_ge(s_hT, i - 1)
                for k in range(n // P):
                    last = nc.tensor.transpose(ps_t[i % 2][:, k * P:(k + 1) * P], m.h[:, i * per + k, :], m.ident[:, :])
                last.then_inc(s_t, 1)
                if i:
                    product(i - 1)
            product(len(CHUNKS) - 1)

        @block.scalar
        def _(act):
            for i, (c, n) in enumerate(CHUNKS):
                act.wait_ge(s_t, i + 1)
                nc.scalar.activation(m.hT[:, c:c + n], ps_t[i % 2][:, 0:n], ACT.Copy).then_inc(s_hT, 1)

        @block.vector
        def _(dve):
            for i, (c, n) in enumerate(CHUNKS):
                k = n // P
                dve.wait_ge(s_h, i + 1)
                nc.vector.tensor_copy(half[:, i * per:i * per + k, :], ps_h[i % 2][:, 0:k, :]).then_inc(s_h_free, 1)


def edge_phase(nc, m, a):
    with ExitStack() as ctx:
        def sb(name, shape, dt):
            return ctx.enter_context(nc.sbuf_tensor(f"edge_{name}", shape, dt))

        def sem(name):
            return ctx.enter_context(nc.semaphore(f"edge_{name}"))

        lane = sb("lane", [P, P], F32)
        wd = sb("wd", [GT * D, GT, HID], F32)
        pay = sb("pay", [P, GT, PAY], F32)
        attr = sb("attr", [P, GT, D], F32)
        dstf = sb("dstf", [P, GT], F32)
        dst = sb("dst", [P, GT], I32)
        half = sb("half", [P, GT, HID], F32)
        attrT = sb("attrT", [GT * D, P], F32)
        hid = sb("hid", [P, GT, HID], F32)
        hot = sb("hot", [P, GT, P], F32)
        rel = sb("rel", [P, GT], F32)
        base = sb("base", [P, 1], F32)
        inv = sb("inv", [P, NB], F32)
        ps_t = ctx.enter_context(nc.psum_tensor("edge_ps_t", [GT * D, P], F32))
        ps_h = [ctx.enter_context(nc.psum_tensor(f"edge_ps_h{j}", [P, HID], F32)) for j in range(GT)]
        ps_s = ctx.enter_context(nc.psum_tensor("edge_ps_s", [P, HID], F32))

        s_const, s_w, s_load, s_inv = sem("s_const"), sem("s_w"), sem("s_load"), sem("s_inv")
        s_pay = [sem(f"s_pay_{e}") for e in ("pool", "dve")]
        s_pay_free = [sem(f"s_pay_free_{e}") for e in ("pool", "dve")]
        s_attr, s_attr_free = sem("s_attr"), sem("s_attr_free")
        s_dst, s_half_free, s_rel = sem("s_dst"), sem("s_half_free"), sem("s_rel")
        s_half = [sem(f"s_half{j}") for j in range(GT)]
        s_t, s_attrT, s_h, s_hid, s_hot, s_hot_free = (sem(n) for n in ("s_t", "s_attrT", "s_h", "s_hid", "s_hot", "s_hot_free"))
        s_full, s_read = sem("s_full"), sem("s_read")
        rows = a.sorted.rearrange("(g j p) c -> g p j c", j=GT, p=P)

        def bounds(eng, b):
            return (eng.value_load(m.tab[0:1, SLO, bass.ds(b, 1)], min_val=0, max_val=G - 2),
                    eng.value_load(m.tab[0:1, SHI, bass.ds(b, 1)], min_val=2, max_val=G))

        block = ctx.enter_context(nc.Block())

        @block.sync
        def _(sp):
            sp.wait_ge(s_const, 2)
            for j in range(GT):
                sp.dma_start(wd[j * D:(j + 1) * D, j, :], a.w1a[D:2 * D, :]).then_inc(s_w, 16)
            for s in s_pay_free:
                sp.sem_inc(s, 1)
            with sp.Fori(0, NB) as b:
                lo, hi = bounds(sp, b)
                with sp.Fori(lo, hi) as g:
                    for s in s_pay_free:
                        take(sp, s)
                    sp.dma_start(pay[:, :, :], rows[bass.ds(g, 1)].squeeze(0)).then_inc(s_load, 16)
                    take(sp, s_load, 16)
                    for s in s_pay:
                        sp.sem_inc(s, 1)

        @block.gpsimd
        def _(pool):
            pool.iota(lane[:, :], [[1, P]], base=0, channel_multiplier=0,
                      allow_small_or_imprecise_dtypes=True).then_inc(s_const, 1)
            pool.memset(wd[:, :, :], 0.0).then_inc(s_const, 1)
            with pool.Fori(0, NB) as b:
                lo, hi = bounds(pool, b)
                with pool.Fori(lo, hi):
                    take(pool, s_pay[0])
                    pool.tensor_copy(dstf[:, :], pay[:, :, D]).then_inc(s_dst, 1)
                    take(pool, s_dst)
                    pool.sem_inc(s_pay_free[0], 1)
                    for j in range(GT):
                        if j % 2 == 0:
                            take(pool, s_half_free, 2)
                            pool.tensor_copy(dst[:, j:j + 2], dstf[:, j:j + 2]).then_inc(s_dst, 1)
                            take(pool, s_dst)
                        pool.indirect_dma_start(half[:, j, :], None, a.half,
                                                bass.IndirectOffsetOnAxis(dst[:, j:j + 1], 0)).then_inc(s_half[j], 16)

        @block.vector
        def _(dve):
            v = nc.vector

            def run(ins):
                ins.then_inc(s_rel, 1)
                take(dve, s_rel)

            run(v.tensor_scalar(inv[:, :], m.outdeg[:, :], 1.0, None, ALU.max))
            run(v.reciprocal(inv[:, :], inv[:, :]))
            run(v.tensor_tensor(m.sums[:, :, HID], m.outdeg[:, :], inv[:, :], ALU.mult))
            dve.sem_inc(s_inv, 1)
            run(v.memset(base[:, :], 0.0))
            dve.wait_ge(s_const, 2)
            with dve.Fori(0, NB) as b:
                lo, hi = bounds(dve, b)
                with dve.Fori(lo, hi):
                    take(dve, s_pay[1])
                    take(dve, s_attr_free)
                    v.tensor_copy(attr[:, :, :], pay[:, :, 0:D]).then_inc(s_attr, 1)
                    dve.drain()
                    run(v.tensor_scalar(rel[:, :], pay[:, :, D + 1], base[:, 0:1], None, ALU.subtract))
                    dve.sem_inc(s_pay_free[1], 1)
                    for j in range(GT):
                        take(dve, s_hot_free)
                        v.tensor_scalar(hot[:, j, :], lane[:, :], rel[:, j:j + 1], None, ALU.is_equal).then_inc(s_hot, 1)
                run(v.tensor_scalar(base[:, :], base[:, :], float(P), None, ALU.add))

        @block.scalar
        def _(act):
            act.wait_ge(s_inv, 1)
            with act.Fori(0, NB) as b:
                lo, hi = bounds(act, b)
                with act.Fori(lo, hi):
                    take(act, s_t)
                    nc.scalar.activation(attrT[:, :], ps_t[:, :], ACT.Copy).then_inc(s_attrT, 1)
                    for j in range(GT):
                        take(act, s_h)
                        act.sem_inc(s_half_free, 1)
                        nc.scalar.activation(hid[:, j, :], ps_h[j][:, :], ACT.Relu).then_inc(s_hid, 1)
                take(act, s_full)
                nc.scalar.activation(m.sums[:, bass.ds(b, 1), 0:HID].squeeze(1), ps_s[:, :], ACT.Copy,
                                     scale=inv[:, bass.ds(b, 1)]).then_inc(s_read, 1)

        @block.tensor
        def _(pe):
            got = pe.alloc_register("gathered")
            pe.reg_mov(got, 0)

            def group(first):
                pe.reg_add(got, got, 16)
                count = pe.snap(got, min_val=16, max_val=16 * G * NB)

                def segment(j):
                    take(pe, s_hot)
                    take(pe, s_hid)
                    nc.tensor.matmul(ps_s[:, :], hot[:, j, :], hid[:, j, :], start=first and j == 0, stop=True,
                                     skip_group_check=True).then_inc(s_hot_free, 1)

                take(pe, s_attr)
                nc.tensor.transpose(ps_t[:, :], attr[:, :, :].rearrange("p j c -> p (j c)"), m.ident[:, :]).then_inc(s_t, 1)
                take(pe, s_attrT)
                pe.sem_inc(s_attr_free, 1)
                for j in range(GT):
                    nc.tensor.matmul(ps_h[j][:, :], attrT[:, :], wd[:, j, :], start=True, stop=False)
                for j in range(GT):
                    pe.wait_ge(s_half[j], count)
                    nc.tensor.matmul(ps_h[j][:, :], m.ident[:, :], half[:, j, :], start=False, stop=True).then_inc(s_h, 1)
                    if j:
                        segment(j - 1)
                segment(GT - 1)

            pe.sem_inc(s_attr_free, 1)
            pe.sem_inc(s_half_free, GT)
            pe.sem_inc(s_hot_free, GT)
            pe.wait_ge(s_w, 16 * GT)
            with pe.Fori(0, NB) as b:
                lo, hi = bounds(pe, b)
                group(True)
                with pe.Fori(lo + 1, hi):
                    group(False)
                pe.drain().then_inc(s_full, 1)
                take(pe, s_read)


def output_phase(nc, m, a, out):
    with ExitStack() as ctx:
        def sb(name, shape, dt):
            return ctx.enter_context(nc.sbuf_tensor(f"outp_{name}", shape, dt))

        def sem(name):
            return ctx.enter_context(nc.semaphore(f"outp_{name}"))

        w1b = sb("w1b", [HID + 1, HID], F32)
        w2x = sb("w2x", [D, HID], F32)
        w2g = sb("w2g", [HID, HID], F32)
        b2a = sb("b2a", [HID, 1], F32)
        w2b = sb("w2b", [HID, D], F32)
        b2b = sb("b2b", [1, D], F32)
        sumT = sb("sumT", [HID + 1, 2, BANK], F32)
        aggT = sb("aggT", [HID, 2, BANK], F32)
        hidT = sb("hidT", [HID, 2, BANK], F32)
        ps_t = [ctx.enter_context(nc.psum_tensor(f"outp_ps_t{i}", [HID + 1, BANK], F32)) for i in range(2)]
        ps_g = [ctx.enter_context(nc.psum_tensor(f"outp_ps_g{i}", [HID, BANK], F32)) for i in range(2)]
        ps_h = [ctx.enter_context(nc.psum_tensor(f"outp_ps_h{i}", [HID, BANK], F32)) for i in range(2)]
        ps_o = [ctx.enter_context(nc.psum_tensor(f"outp_ps_o{i}", [P, BANK // P, D], F32)) for i in range(2)]
        s_w, s_t, s_sumT, s_g, s_aggT, s_h, s_hidT, s_o, s_x, s_out = (
            sem(n) for n in ("s_w", "s_t", "s_sumT", "s_g", "s_aggT", "s_h", "s_hidT", "s_o", "s_x", "s_out"))
        per = BANK // P
        NC = len(CHUNKS)
        block = ctx.enter_context(nc.Block())

        @block.sync
        def _(sp):
            def row(v):
                return v.rearrange("(a n) -> a n", a=1)
            loads = ((w1b[0:HID, :], a.w1b), (w1b[HID:HID + 1, :], row(a.b1b)), (w2x[:, :], a.w2a[0:D, :]),
                     (w2g[:, :], a.w2a[D:D + HID, :]), (b2a[:, :], a.b2a.rearrange("(n a) -> n a", a=1)),
                     (w2b[:, :], a.w2b), (b2b[:, :], row(a.b2b)))
            for to, of in loads:
                sp.dma_start(to, of).then_inc(s_w, 16)
            full = NODES // P
            sp.wait_ge(s_x, NC)
            sp.dma_start(out[0:full * P, :].rearrange("(h p) c -> p h c", p=P), m.x[:, 0:full, :]).then_inc(s_out, 16)
            sp.dma_start(out[full * P:NODES, :], m.x[0:NODES - full * P, full, :]).then_inc(s_out, 16)
            sp.wait_ge(s_out, 32)

        @block.tensor
        def _(pe):
            pe.wait_ge(s_w, 16 * 7)
            for i in range(NC + 3):
                if i < NC:
                    c, n = CHUNKS[i]
                    if i >= 2:
                        pe.wait_ge(s_sumT, i - 1)
                    for k in range(n // P):
                        last = nc.tensor.transpose(ps_t[i % 2][:, k * P:(k + 1) * P], m.sums[:, i * per + k, :],
                                                   m.ident[:, :])
                    last.then_inc(s_t, 1)
                if 0 <= i - 1 < NC:
                    j = i - 1
                    n = CHUNKS[j][1]
                    pe.wait_ge(s_sumT, j + 1)
                    if j >= 2:
                        pe.wait_ge(s_aggT, j - 1)
                    nc.tensor.matmul(ps_g[j % 2][:, 0:n], w1b[:, :], sumT[:, j % 2, 0:n], start=True,
                                     stop=True).then_inc(s_g, 1)
                if 0 <= i - 2 < NC:
                    j = i - 2
                    c, n = CHUNKS[j]
                    pe.wait_ge(s_aggT, j + 1)
                    if j >= 2:
                        pe.wait_ge(s_hidT, j - 1)
                    nc.tensor.matmul(ps_h[j % 2][:, 0:n], w2g[:, :], aggT[:, j % 2, 0:n], start=True, stop=False)
                    nc.tensor.matmul(ps_h[j % 2][:, 0:n], w2x[:, :], m.hT[:, c:c + n], start=False,
                                     stop=True).then_inc(s_h, 1)
                if 0 <= i - 3 < NC:
                    j = i - 3
                    pe.wait_ge(s_hidT, j + 1)
                    if j >= 2:
                        pe.wait_ge(s_x, j - 1)
                    for k in range(CHUNKS[j][1] // P):
                        nc.tensor.matmul(ps_o[j % 2][:, k, :], hidT[:, j % 2, k * P:(k + 1) * P], w2b[:, :],
                                         start=True, stop=False)
                        last = nc.tensor.matmul(ps_o[j % 2][:, k, :], m.ones[:, :], b2b[:, :], start=False, stop=True)
                    last.then_inc(s_o, 1)

        @block.scalar
        def _(act):
            act.wait_ge(s_w, 16 * 7)
            for i in range(NC + 2):
                if i < NC:
                    act.wait_ge(s_t, i + 1)
                    if i >= 2:
                        act.wait_ge(s_g, i - 1)
                    n = CHUNKS[i][1]
                    nc.scalar.activation(sumT[:, i % 2, 0:n], ps_t[i % 2][:, 0:n], ACT.Copy).then_inc(s_sumT, 1)
                if 0 <= i - 2 < NC:
                    j = i - 2
                    n = CHUNKS[j][1]
                    act.wait_ge(s_h, j + 1)
                    if j >= 2:
                        act.wait_ge(s_o, j - 1)
                    nc.scalar.activation(hidT[:, j % 2, 0:n], ps_h[j % 2][:, 0:n], ACT.Relu,
                                         bias=b2a[:, 0:1]).then_inc(s_hidT, 1)

        @block.vector
        def _(dve):
            def result(j):
                c, n = CHUNKS[j]
                h = m.x[:, j * per:j * per + n // P, :]
                dve.wait_ge(s_o, j + 1)
                nc.vector.tensor_tensor(h, ps_o[j % 2][:, 0:n // P, :], h, ALU.add).then_inc(s_x, 1)

            for i in range(NC + 2):
                if i < NC:
                    n = CHUNKS[i][1]
                    dve.wait_ge(s_g, i + 1)
                    if i >= 2:
                        dve.wait_ge(s_h, i - 1)
                    nc.vector.tensor_copy(aggT[:, i % 2, 0:n], ps_g[i % 2][:, 0:n]).then_inc(s_aggT, 1)
                if i >= 2:
                    result(i - 2)


def program(nc, a, out):
    with ExitStack() as ctx:
        def sb(name, shape, dt, where=ctx):
            return where.enter_context(nc.sbuf_tensor(name, shape, dt))

        m = Mem()
        m.ident = sb("ident", [P, P], F32)
        m.identb = sb("identb", [P, P], BF16)
        m.ones = sb("ones_row", [1, P], F32)
        m.zero = sb("zero", [P, NB], F32)
        m.x = sb("x", [P, NB, D], F32)
        m.beta = sb("beta", [D, 1], F32)
        m.ends = sb("ends", [P, T, 2], I16)
        m.tab = sb("tab", [P, 4, NB], I32)
        m.col = sb("col", [P, 2], F32)
        m.mean = sb("mean", [P, NB], F32)
        m.var = sb("var", [P, NB], F32)
        m.root = sb("root", [P, NB], F32)
        m.inv = sb("inv", [P, NB], F32)
        m.t25 = sb("t25", [P, NB], F32)
        m.indeg7 = sb("indeg7", [P, NB * len(CHUNKS)], F32)
        m.outdeg = sb("outdeg", [P, NB], F32)
        m.hw = sb("hw", [P, NB, D + 1], F32)
        with ExitStack() as adj:
            m.nT = sb("nT", [D, NP], F32)
            with ExitStack() as early:
                m.cols = sb("cols", [P, NP], I16, early)
                m.pos = sb("pos", [P, T], I32, early)
                with ExitStack() as now:
                    m.h = sb("h0", [P, NB, D], F32, now)
                    m.sq = sb("sq0", [P, NB, D], F32, now)
                    setup_phase(nc, m, a)
                adjacency_phase(nc, m, a)
            m.adjT = sb("adjT", [P, NB, NP], BF16, adj)
            attention_phase(nc, m, a)
            with ExitStack() as now:
                m.h = sb("h1", [P, NB, D], F32, now)
                norm_phase(nc, m, a.h, "norm1")
            convolution_phase(nc, m, a)
            with ExitStack() as now:
                m.h = sb("h2", [P, NB, D], F32, now)
                norm_phase(nc, m, None, "norm2")
                propagation_phase(nc, m, a)
        m.hT = sb("hT", [D, NP], F32)
        m.sums = sb("sums", [P, NB, HID + 1], F32)
        with ExitStack() as now:
            m.h = sb("h3", [P, NB, D], F32, now)
            norm_phase(nc, m, None, "norm3")
            node_half_phase(nc, m, a)
        edge_phase(nc, m, a)
        output_phase(nc, m, a, out)


def kernel(x, src, dst, edge_attr_3, edge_attr_32, L0_gnn_beta, L1_gnn_W, L1_gnn_b, L3_gnn_u, L3_gnn_W1a, L3_gnn_b1a,
           L3_gnn_W1b, L3_gnn_b1b, L3_gnn_W2a, L3_gnn_b2a, L3_gnn_W2b, L3_gnn_b2b):
    import numpy as np
    import concourse.bacc as bacc
    from concourse.bass_utils import run_bass_kernel_spmd as run
    nc = bacc.Bacc("TRN2", target_bir_lowering=False, num_devices=1)

    def padded(v, rows, fill=0):
        v = np.asarray(v)
        return np.concatenate([v, np.full((rows - v.shape[0],) + v.shape[1:], fill, v.dtype)])

    arrays = {"x": padded(x, NP), "src": padded(src, EP, NP - 1), "dst": padded(dst, EP, NP - 1),
              "vec": padded(edge_attr_3, EP), "attr": padded(edge_attr_32, EP), "beta": L0_gnn_beta,
              "w1": L1_gnn_W, "b1": L1_gnn_b, "w1a": L3_gnn_W1a, "b1a": L3_gnn_b1a, "w1b": L3_gnn_W1b,
              "b1b": L3_gnn_b1b, "w2a": L3_gnn_W2a, "b2a": L3_gnn_b2a, "w2b": L3_gnn_W2b, "b2b": L3_gnn_b2b}
    arrays = {n: np.ascontiguousarray(v) for n, v in arrays.items()}

    def given(n):
        return nc.dram_tensor(f"{n}_in", arrays[n].shape, mybir.dt.from_np(arrays[n].dtype), kind="ExternalInput").ap()

    def scratch(n, shape, dt):
        return nc.dram_tensor(n, shape, dt, kind="Internal").ap()

    a = Mem()
    a.x, a.src, a.dst, a.vec, a.attr, a.beta, a.w1, a.b1 = (
        given(n) for n in ("x", "src", "dst", "vec", "attr", "beta", "w1", "b1"))
    a.w1a, a.b1a, a.w1b, a.b1b, a.w2a, a.b2a, a.w2b, a.b2b = (
        given(n) for n in ("w1a", "b1a", "w1b", "b1b", "w2a", "b2a", "w2b", "b2b"))
    a.sh = scratch("harmonics", (P, T * NSH), F32)
    a.adj = scratch("adjacency", (NP, NP), BF16)
    a.sorted = scratch("sorted_edges", (EP, PAY), F32)
    a.h = scratch("features", (NP, D), F32)
    a.half = scratch("half_rows", (NP, HID), F32)
    out = nc.dram_tensor("out", (NODES, D), F32, kind="ExternalOutput").ap()
    program(nc, a, out)
    return run(nc, [{f"{n}_in": v for n, v in arrays.items()}], core_ids=[0]).results[0]["out"]
```
